# Optimizing a Trainium2 kernel written in Bass

```python
import numpy as np
import jax
import jax.numpy as jnp

def _softmax(x, axis=-1):
    return jax.nn.softmax(x, axis=axis)

def _gelu(x):
    return jax.nn.gelu(x, approximate=True)

def _silu(x):
    return jax.nn.silu(x)

def _sigmoid(x):
    return jax.nn.sigmoid(x)

def _layernorm(x, axis=-1, eps=1e-05):
    m = jnp.mean(x, axis=axis, keepdims=True)
    v = jnp.var(x, axis=axis, keepdims=True)
    return (x - m) / jnp.sqrt(v + eps)

def _scatter_add(tgt, idx, src, axis=0):
    return tgt.at[idx].add(src)

def _segment_sum(src, seg, n):
    return jax.ops.segment_sum(src, seg, n)
kernel_name = 'mk_gnn_resnorm_d2_gnn_r32_a7e0e7'

def setup_inputs(seed: int=0):
    np.random.seed(seed)
    _w = jnp.asarray

    def _rec_inputs():
        import jax
        import jax.numpy as jnp
        _gk = jax.random.key(seed)
        x = -0.0002117 + 1 * jax.random.normal(jax.random.fold_in(_gk, 1), (3125, 256), jnp.float32)
        src = jax.random.randint(jax.random.fold_in(_gk, 2), (50000,), 0, 3125, jnp.int32)
        dst = jnp.minimum((3125 * jax.random.uniform(jax.random.fold_in(_gk, 3), (50000,)) ** 2.0).astype(jnp.int32), 99999)
        _o = jnp.argsort(dst, stable=True)
        src = src[_o]
        dst = dst[_o]
        edge_weight = jax.random.uniform(jax.random.fold_in(_gk, 13), (50000,), jnp.float32, 0.0, 1)
        return (x, src, dst, edge_weight)
    x, src, dst, edge_weight = _rec_inputs()

    def _L0_gnn_setup():
        import jax, jax.numpy as jnp
        import numpy as np
        N_NODES = 3125
        N_EDGES = 100000
        D_IN = 256
        D_OUT = 256
        key = jax.random.key(seed)
        k1, k2, k3, k4, k5 = jax.random.split(key, 5)
        X = jax.random.normal(k1, (N_NODES, D_IN), dtype=jnp.float32)
        edge_row = jax.random.randint(k2, (N_EDGES,), 0, N_NODES, dtype=jnp.int32)
        edge_col = jax.random.randint(k3, (N_EDGES,), 0, N_NODES, dtype=jnp.int32)
        edge_val = jax.random.uniform(k4, (N_EDGES,), dtype=jnp.float32)
        W = jax.random.normal(k5, (D_OUT, D_IN), dtype=jnp.float32) * (6.0 / (D_IN + D_OUT)) ** 0.5
        b = jnp.zeros((D_OUT,), dtype=jnp.float32)
        return {'X': X, 'edge_row': edge_row, 'edge_col': edge_col, 'edge_val': edge_val, 'W': W, 'b': b}
    _L0_gnn_all = _L0_gnn_setup()
    _L0_gnn_in = {k: v for k, v in _L0_gnn_all.items() if k in ('W', 'b')}
    del _L0_gnn_all

    def _L1_gnn_setup():
        import jax, jax.numpy as jnp
        import numpy as np
        N_NODES = 50000
        N_EDGES = 9375
        DIM = 256
        ALPHA = 0.1

        def gcn_layer(x0, x, edge_idx, W):
            src, dst = (edge_idx[0], edge_idx[1])
            msgs = x[src]
            agg = jax.ops.segment_sum(msgs, dst, num_segments=x.shape[0])
            deg = jax.ops.segment_sum(jnp.ones((src.shape[0],), x.dtype), dst, num_segments=x.shape[0])
            agg = agg / jnp.maximum(deg, 1.0)[:, None]
            h = ALPHA * x0 + (1.0 - ALPHA) * agg
            return h @ W
        key = jax.random.key(seed)
        k1, k2, k3 = jax.random.split(key, 3)
        x = jax.random.normal(k1, (N_NODES, DIM), dtype=jnp.float32)
        edge_idx = jax.random.randint(k2, (2, N_EDGES), 0, N_NODES, dtype=jnp.int64)
        W = jax.random.normal(k3, (DIM, DIM), dtype=jnp.float32) / np.sqrt(DIM)
        return {'drug_cell_pair_feature': x, 'edge_idx': edge_idx, 'W': W}
    _L1_gnn_all = _L1_gnn_setup()
    _L1_gnn_in = {k: v for k, v in _L1_gnn_all.items() if k in ('W',)}
    del _L1_gnn_all
    return {'x': x, 'src': src, 'dst': dst, 'edge_weight': edge_weight, 'L0_gnn_W': _L0_gnn_in['W'], 'L0_gnn_b': _L0_gnn_in['b'], 'L1_gnn_W': _L1_gnn_in['W']}

def reference(x, src, dst, edge_weight, L0_gnn_W, L0_gnn_b, L1_gnn_W):
    import jax
    import jax.numpy as jnp

    def _L0_gnn_ref(X, edge_row, edge_col, edge_val, W, b):
        import jax, jax.numpy as jnp
        import numpy as np
        N_NODES = 3125
        N_EDGES = 100000
        D_IN = 256
        D_OUT = 256
        msgs = edge_val[:, None] * X[edge_col]
        h = jax.ops.segment_sum(msgs, edge_row, num_segments=N_NODES)
        return h @ W.T + b

    def _L1_gnn_ref(drug_cell_pair_feature, edge_idx, W):
        import jax, jax.numpy as jnp
        import numpy as np
        N_NODES = 50000
        N_EDGES = 9375
        DIM = 256
        ALPHA = 0.1

        def gcn_layer(x0, x, edge_idx, W):
            src, dst = (edge_idx[0], edge_idx[1])
            msgs = x[src]
            agg = jax.ops.segment_sum(msgs, dst, num_segments=x.shape[0])
            deg = jax.ops.segment_sum(jnp.ones((src.shape[0],), x.dtype), dst, num_segments=x.shape[0])
            agg = agg / jnp.maximum(deg, 1.0)[:, None]
            h = ALPHA * x0 + (1.0 - ALPHA) * agg
            return h @ W
        x0 = drug_cell_pair_feature
        out = jax.nn.relu(gcn_layer(x0, x0, edge_idx, W))
        for _ in range(4):
            out = jax.nn.relu(gcn_layer(x0, out, edge_idx, W))
        return out
    edge_index = jnp.stack([src, dst])
    x = _layernorm(x + _L0_gnn_ref(x, src, dst, edge_weight, L0_gnn_W, L0_gnn_b), axis=-1)
    x = _layernorm(x + _L1_gnn_ref(x, edge_index, L1_gnn_W), axis=-1)
    return x

_drawn_inputs = setup_inputs


def setup_inputs(seed=0):
    import zlib

    import numpy as np

    out = dict(_drawn_inputs(seed))
    spreads = {'L0_gnn_b': (0.0, 0.306)}
    factors = {}
    for name, (base, spread) in spreads.items():
        noise = np.random.default_rng([zlib.crc32(name.encode()), seed]).standard_normal(out[name].shape)
        drawn = base * np.exp(spread * noise) if base else spread * noise
        out[name] = jnp.asarray(drawn.astype(out[name].dtype))
    for name, factor in factors.items():
        out[name] = (out[name] * factor).astype(out[name].dtype)
    return out
```

```python
import concourse.bass as bass
from concourse import mybir


def gnn_resnorm_kernel(
    nc: bass.Bass,
    x: bass.AP,
    src: bass.AP,
    dst: bass.AP,
    edge_weight: bass.AP,
    W0: bass.AP,
    b0: bass.AP,
    W1: bass.AP,
    out: bass.AP,
):
    F32, F16, BF16, I32, U16 = (mybir.dt.float32, mybir.dt.float16, mybir.dt.bfloat16, mybir.dt.int32, mybir.dt.uint16)
    ALU, ACT, AX = mybir.AluOpType, mybir.ActivationFunctionType, mybir.AxisListType

    P = 128
    N, D = x.shape
    E = src.shape[0]
    NB = -(-N // P)
    TAIL = N - (NB - 1) * P
    KC = D // P
    WIN = 16
    WPB = P // WIN
    NW = NB * WPB
    NWP = NW + 2
    KM = 32
    ROW = 4 * P
    NR = -(-E // ROW)
    NCH = 4 * NR
    NCHP = NCH + 4
    REST = E - (NR - 1) * ROW
    HW = NW // 2
    ROUND = 1.5 * 2 ** 23
    FAR = 4095
    ALPHA, EPS, LAYERS = 0.1, 1e-5, 5
    FURTHER = 2
    Q = 2
    WL_DVE = 1
    G = 5
    assert NB % G == 0 and NB <= KM and KC == 2 and NW * WIN <= FAR and NCH - 1 + Q <= NCHP and LAYERS % 2 == 1

    at = [(nc.sbuf_base + 63) // 64 * 64]

    def place(name, shape, dtype, offset=None):
        size = 4 if dtype in (F32, I32) else 2
        for n in shape[1:]:
            size *= n
        size = (size + 31) // 32 * 32
        if offset is None:
            offset = at[0]
            at[0] += size
        return nc.alloc_sbuf_tensor_at(name, list(shape), dtype, offset=offset), offset + size

    adj_start = at[0]
    adj, adj_end = place("adj", (P, NB, NB, P), F16)
    BLOCK, WBLOCK, YBLOCK = NB * P * 2, 2 * NB * P * 2, 2 * D * 2
    LAG = (adj_end - adj_start - WBLOCK) // BLOCK - 1
    wadj1_start = adj_end - WBLOCK
    Y_IN = (wadj1_start - YBLOCK - adj_start) // BLOCK - 1
    y_start = wadj1_start - Y_IN * YBLOCK
    Y_GAP = WBLOCK // (YBLOCK // 2)
    y, y_end = place("y", (P, 2 * NB + Y_GAP, D), F16, y_start)

    def y_at(d):
        at_d = d * 2 + ((d + (32 - Y_IN)) >> 5) * Y_GAP
        return at_d if isinstance(at_d, int) else at_d.with_bounds(min_val=0, max_val=2 * NB + Y_GAP - 2)

    assert NB <= 32 and WBLOCK % (YBLOCK // 2) == 0 and LAG % 2 == 0 and WPB == 8
    for d in range(1, Y_IN + 1):
        assert y_start + (d - 1) * YBLOCK >= adj_start + (d + 1) * BLOCK
    at[0] = (adj_end + 31) // 32 * 32
    z_start = at[0]
    ZW = 2 * D + 2
    z, z_end = place("z", (P, 2 * NB, ZW), F16)
    h_start = (z_start + NB * ZW * 2 + 31) // 32 * 32
    h, _ = place("h", (P, NB, D), F32, h_start)
    wadj0, o = place("wadj0", (P, 2, NB, P), F16, y_end)
    wadj1, _ = place("wadj1", (P, 2, NB, P), F16, wadj1_start)
    wadj = [wadj0, wadj1]
    lo_rows = [place("lo_rows0", (P, Q, 3, P), F16, o)]
    key_rows = [place("key_rows0", (P, Q, NB, WIN), F16, lo_rows[0][1])]
    o = key_rows[0][1]
    wadjT, o = place("wadjT", (P, 2, 2, 2, P), F16, o)
    bounds, o = place("bounds", (1, NWP + 2, 4), U16, o)
    win_key, o = place("win_key", (P, NWP, 4), BF16, o)
    iota_lo, o = place("iota_lo", (P, P), F16, o)
    scal, o = place("scal", (P, 3, Q, 4), F32, o)
    assert o <= h_start
    w0, o = place("w0", (P, KC, D), F32, y_end)
    w0T, o = place("w0T", (P, KC, 2, D), F16, o)
    bias, o = place("bias", (P, D), F32, o)
    dst_raw, o = place("dst_raw", (P, ROW), I32, adj_start)
    src_raw, o = place("src_raw", (P, ROW), I32, o)
    wgt_raw, o = place("wgt_raw", (P, ROW), F32, o)
    src_hi, o = place("src_hi", (P, ROW), I32, o)
    src_lo, o = place("src_lo", (P, ROW), I32, o)
    dst_win, o = place("dst_win", (P, ROW), I32, o)
    key_f, o = place("key_f", (P, ROW), F32, o)
    src_lo_f, o = place("src_lo_f", (P, ROW), F32, o)
    chunk_rng, o = place("chunk_rng", (P, 2, 4), F32, o)
    ones16, o = place("ones16", (P, P), F16, o)
    rng_rows, o = place("rng_rows", (P, 2, 4, P), F16, o)
    chunk_no, o = place("chunk_no", (P, 2, 4, NR), F32, o)
    win_no, o = place("win_no", (P, 2), F32, o)
    active, o = place("active", (P, 2, NCH), F32, o)
    cand, o = place("cand", (P, 2, NCH), F32, o)
    win_rng, o = place("win_rng", (P, 2, 2), F32, o)
    win_rng16, o = place("win_rng16", (P, 2, 2), F16, o)
    win_row, o = place("win_row", (1, 2, NW), F32, o)
    steps_row, o = place("steps_row", (1, 3, NWP), F32, o)
    wh16, o = place("wh16", (P, NR, 4), F16, o)
    assert o <= y_start
    identf, _ = place("identf", (P, P), F32)
    identh, _ = place("identh", (P, P), F16)
    shared = at[0]
    outT, outT_end = place("outT", (P, 2, 2, KC, P), F16, shared)
    o = shared
    for n in (1, 2):
        for rows, name, shape in ((lo_rows, "lo_rows", (P, Q, 3, P)), (key_rows, "key_rows", (P, Q, NB, WIN))):
            t, o = place(f"{name}{n}", shape, F16, o)
            rows.append((t, o))
    lo_rows, key_rows = [t for t, _ in lo_rows], [t for t, _ in key_rows]
    tab, o = place("tab", (P, NCHP, 4), F32, o)
    iota_key, o = place("iota_key", (P, NB, WIN), F16, o)
    assert o <= nc.sbuf_usable_end
    w1s, o = place("w1s", (P, KC, 2, D), F16, outT_end)
    outb, o = place("outb", (P, D), F32, o)
    pre, o = place("pre", (P, D), F32, o)
    base_ring, o = place("base_ring", (P, G, D), F32, o)
    w1 = base_ring[:, 0:KC, :]
    scale, o = place("scale", (P, 2), F32, o)
    stat, o = place("stat", (P, G, 6), F32, o)
    mean_var, o = place("mean_var", (P, NB, 2), F32, o)
    ln, o = place("ln", (P, 4, G), F32, o)
    rstd, o = place("rstd", (P, NB), F32, o)
    assert o <= nc.sbuf_usable_end

    x1_dram = nc.dram_tensor("x1_scratch", [P, NB, D], F32).ap()
    base_dram = nc.dram_tensor("base_scratch", [NB, P, D], F32).ap()

    ps = nc.alloc_psum_tensor("ps", [P, 8, 512], F32)
    CNT, WGT, TRB, L0B = 0, 2, (4, 7), 5
    AGG, ZB = 0, 6
    TB, TB_LAYERS = (5, 4), (5, 5)
    NPAIR = (NB + 1) // 2
    PAIRS = [range(max(2 * k - 1, 0), min(2 * k + 1, NPAIR)) for k in range(WPB)]
    assert PAIRS[-1].stop == NPAIR
    trh = [ps[:, bank, :].bitcast(F16).rearrange("p (s h c) -> p s h c", s=4, h=2)[:, 0:2] for bank in TRB]

    def sem(name):
        return nc.alloc_semaphore(name)

    edges_in, w0_in, w1_in, bias_in, x_in = sem("edges_in"), sem("w0_in"), sem("w1_in"), sem("bias_in"), sem("x_in")
    raw_cleared, tail_cleared, consts_made, dve_consts = sem("raw_cleared"), sem("tail_cleared"), sem("consts_made"), sem("dve_consts")
    dve_chain, pool_chain = sem("dve_chain"), sem("pool_chain")
    edges_split, edges_turned, w0_turned, w0_copied, w0_split, w1_copied, w1_split = (
        sem(n) for n in ("edges_split", "edges_turned", "w0_turned", "w0_copied", "w0_split", "w1_copied", "w1_split"))
    rows_made, rows_spread, win_found, win_turned, bounds_made = (
        sem(n) for n in ("rows_made", "rows_spread", "win_found", "win_turned", "bounds_made"))
    bias_added, tab_used = sem("bias_added"), sem("tab_used")
    x1_ready, turned, hi_split, lo_split, product, z_hi, z_lo = (
        sem(n) for n in ("x1_ready", "turned", "hi_split", "lo_split", "product", "z_hi", "z_lo"))
    scal_ready, lo_made, key_made, wh_made, wl_made, rows_used = (
        [[sem(f"{n}{side}{q}") for q in range(Q)] for side in ("_even", "_odd", "_further")]
        for n in ("scal_ready", "lo_made", "key_made", "wh_made", "wl_made", "rows_used"))
    cnt_copied, wgt_hi, wgt_copied = sem("cnt_copied"), sem("wgt_hi"), sem("wgt_copied")
    wadj_turned, wadjT_copied, l0_done, l0_added = (
        sem(n) for n in ("wadj_turned", "wadjT_copied", "l0_done", "l0_added"))
    var_ready, std_ready, rstd_made, base_written = (
        sem(n) for n in ("var_ready", "std_ready", "rstd_made", "base_written"))
    agg_done, deg_read, scale_made, agg_read, relu_done, normed = (
        sem(n) for n in ("agg_done", "deg_read", "scale_made", "agg_read", "relu_done", "normed"))
    base_stored = [sem(f"base_stored{j}") for j in range(G)]
    base_loaded = [sem(f"base_loaded{j}") for j in range(G)]
    x1_stored, x1_loaded, out_stored, ones_made = sem("x1_stored"), sem("x1_loaded"), sem("out_stored"), sem("ones_made")
    BIAS = {turned: 1, lo_split: 1, product: 1, z_hi: 1, z_lo: 1, hi_split: 1, x1_ready: 1,
            cnt_copied: 2, wgt_copied: 2, wgt_hi: 1, wadj_turned: 1, wadjT_copied: 1, l0_done: 1, l0_added: 1,
            agg_done: 1, deg_read: 1, scale_made: 1, agg_read: G, relu_done: 1, base_written: 1}
    step_sems = scal_ready, lo_made, key_made, wh_made, wl_made, rows_used
    BIAS.update({s: 1 for kind in step_sems for side in kind for s in side})

    def count(s, n):
        return BIAS[s] + n

    def start(eng, *sems):
        for s in sems:
            eng.sem_inc(s, BIAS[s])

    def slot_free(item, j):
        return item if j == 0 else item - 1

    def window_registers(eng, name):
        return [eng.alloc_register(f"{name}{i}") for i in range(8)]

    def load_windows(eng, regs, w, n=2):
        eng.load(regs[:4 * n], bounds[0:1, bass.ds(w + 1, n), 0:4].rearrange("o w k -> o (w k)"))
        most = NWP * NCH // Q
        return [(eng.snap(regs[i], min_val=0, max_val=most), eng.snap(regs[i + 1], min_val=0, max_val=most),
                 eng.snap(regs[i + 2], min_val=0, max_val=NCH)) for i in range(0, 4 * n, 4)]

    def all_steps(eng, pair, side, window, one_step):
        one_step(side, eng.snap(pair + 1), eng.snap(pair + 2), None)
        with eng.If(window[0] < window[1]):
            with eng.Fori(window[0], window[1]) as step:
                one_step(FURTHER, eng.snap(step + 1), eng.snap(step + 2), step)

    with nc.Block() as block:

        @block.sync
        def _(sp):
            sp.wait_ge(raw_cleared, 3)
            for raw, given in ((dst_raw, dst), (src_raw, src), (wgt_raw, edge_weight)):
                full = (NR - 1) * ROW
                sp.dma_start(raw[0:NR - 1, :], given[0:full].rearrange("(r e) -> r e", e=ROW)).then_inc(edges_in, 16)
                sp.dma_start(raw[NR - 1:NR, 0:REST], given[full:E].rearrange("(r e) -> r e", r=1)).then_inc(edges_in, 16)
            sp.dma_start(w0[:], W0.rearrange("(c p) i -> p c i", p=P)).then_inc(w0_in, 16)
            sp.wait_ge(tail_cleared, 1)
            sp.dma_start(h[:, 0:NB - 1, :], x[0:(NB - 1) * P, :].rearrange("(b p) d -> p b d", p=P)).then_inc(x_in, 16)
            sp.dma_start(h[0:TAIL, NB - 1, :], x[(NB - 1) * P:N, :]).then_inc(x_in, 16)
            sp.dma_start(bias[:], b0.rearrange("(o d) -> o d", o=1).broadcast_to([P, D])).then_inc(bias_in, 16)
            sp.wait_ge(tab_used, 1)
            sp.dma_start(w1, W1.rearrange("(c p) i -> p c i", p=P)).then_inc(w1_in, 16)
            with sp.Fori(0, NB // G) as it:
                sp.wait_ge(x1_ready, count(x1_ready, G * (it + 1)))
                sp.dma_start(x1_dram[:, bass.ds(it * G, G), :], h[:, bass.ds(it * G, G), :]).then_inc(x1_stored, 16)
                for j in range(G):
                    sp.wait_ge(base_written, count(base_written, it * G + j + 1))
                    sp.dma_start(base_dram[it * G + j], base_ring[:, j, :]).then_inc(base_stored[j], 16)
            for j in range(G):
                sp.wait_ge(base_stored[j], 16 * (NB // G))
            def load_bases(layer):
                with sp.Fori(0, NB // G) as it:
                    for j in range(G):
                        sp.wait_ge(agg_read, layer * NB + it * G + j + 1)
                        sp.dma_start(base_ring[:, j, :], base_dram[it * G + j]).then_inc(base_loaded[j], 16)

            with sp.Fori(0, LAYERS - 1) as layer:
                load_bases(layer)
            sp.wait_ge(x1_stored, 16 * (NB // G))
            sp.wait_ge(agg_done, count(agg_done, (LAYERS - 1) * NB))
            sp.dma_start(h[:], x1_dram).then_inc(x1_loaded, 16)
            load_bases(LAYERS - 1)
            for g in range(NB // G):
                sp.wait_ge(normed, g + 1)
                last = min((g + 1) * G, NB - 1)
                sp.dma_start(out[g * G * P:last * P, :].rearrange("(b p) d -> p b d", p=P),
                             h[:, g * G:last, :]).then_inc(out_stored, 16)
            sp.dma_start(out[(NB - 1) * P:N, :], h[0:TAIL, NB - 1, :]).then_inc(out_stored, 16)
            sp.wait_ge(out_stored, 16 * (NB // G + 1))

        @block.gpsimd
        def _(pool):
            chain = [0]

            def link(ins):
                chain[0] += 1
                ins.then_inc(pool_chain, 1)
                pool.wait_ge(pool_chain, chain[0])

            start(pool, x1_ready, *scal_ready[0], *scal_ready[1], *scal_ready[2])
            nc.gpsimd.memset(dst_raw[:], FAR).then_inc(raw_cleared, 1)
            nc.gpsimd.memset(src_raw[:], 0).then_inc(raw_cleared, 1)
            nc.gpsimd.memset(wgt_raw[:], 0.0).then_inc(raw_cleared, 1)
            nc.gpsimd.memset(h[:, NB - 1, :], 0.0).then_inc(tail_cleared, 1)
            for ident in (identf, identh):
                link(nc.gpsimd.memset(ident[:], 0.0))
                nc.gpsimd.affine_select(out=ident[:], in_=ident[:], compare_op=ALU.not_equal, fill=1.0, base=0,
                                        pattern=[[-1, P]], channel_multiplier=1).then_inc(consts_made, 1)
            nc.gpsimd.iota(iota_lo[:], pattern=[[1, P]], base=0, channel_multiplier=0,
                           allow_small_or_imprecise_dtypes=True).then_inc(consts_made, 1)
            nc.gpsimd.iota(iota_key[:], pattern=[[1, NB], [KM, WIN]], base=0, channel_multiplier=0,
                           allow_small_or_imprecise_dtypes=True).then_inc(consts_made, 1)
            link(nc.gpsimd.memset(win_key[:], 0.0))
            nc.gpsimd.iota(win_key[:, :, 0], pattern=[[WIN * KM, NWP]], base=0, channel_multiplier=0,
                           allow_small_or_imprecise_dtypes=True).then_inc(consts_made, 1)
            nc.gpsimd.iota(win_no[:], pattern=[[HW, 2]], base=0, channel_multiplier=1,
                           allow_small_or_imprecise_dtypes=True).then_inc(consts_made, 1)
            nc.gpsimd.iota(chunk_no[:, 0], pattern=[[1, 4], [4, NR]], base=-NCH, channel_multiplier=0,
                           allow_small_or_imprecise_dtypes=True).then_inc(consts_made, 1)
            nc.gpsimd.iota(chunk_no[:, 1], pattern=[[1, 4], [4, NR]], base=1, channel_multiplier=0,
                           allow_small_or_imprecise_dtypes=True).then_inc(consts_made, 1)
            pool.wait_ge(bias_in, 16)
            for i in range(NB):
                pool.wait_ge(turned, count(turned, i + 1))
                nc.gpsimd.tensor_tensor(out=h[:, i, :], in0=h[:, i, :], in1=bias[:], op=ALU.add).then_inc(bias_added, 1)
            pool.wait_ge(bounds_made, 1)
            regs = window_registers(pool, "pool_window")

            def window_scalars(w, pair, side, window):
                further, _, chunk0 = window
                shift = pool.snap(chunk0 + Q - further * Q)

                def one_step(s, before, this, step):
                    chunk = chunk0 if step is None else step * Q + shift
                    chunk = pool.snap(chunk.with_bounds(min_val=0, max_val=NCHP - Q))
                    for q in range(Q):
                        pool.wait_ge(key_made[s][q], before)
                        pool.wait_ge(wh_made[s][q], before)
                        pool.wait_ge(wl_made[s][q], before)
                        nc.gpsimd.tensor_tensor(out=scal[:, s, q, :], in0=tab[:, chunk + q, :], in1=win_key[:, w, :],
                                                op=ALU.subtract).then_inc(scal_ready[s][q], 1)

                all_steps(pool, pair, side, window, one_step)

            window_scalars(0, 0, 0, load_windows(pool, regs, 0, 1)[0])
            with pool.Fori(0, NW // 2) as pair:
                odd, even = load_windows(pool, regs, pair * 2 + 1)
                window_scalars(pair * 2 + 1, pair, 1, odd)
                window_scalars(pair * 2 + 2, pair + 1, 0, even)
            for q in range(Q):
                pool.wait_ge(scal_ready[0][q], NWP // 2 + 1)
            pool.nop().then_inc(tab_used, 1)
            for g in range(NB // G):
                pool.wait_ge(rstd_made, g + 1)
                for i in range(g * G, (g + 1) * G):
                    nc.gpsimd.tensor_scalar(h[:, i, :], h[:, i, :], mean_var[:, i, 0:1], rstd[:, i:i + 1],
                                            ALU.subtract, ALU.mult).then_inc(x1_ready, 1)


        def turn_item(item, j, source, tb=TB):
            nc.tensor.wait_ge(lo_split, count(lo_split, slot_free(item, j) if tb is TB else item))
            for k in range(KC):
                last = nc.tensor.transpose(ps[:, tb[j % 2], k * P:(k + 1) * P],
                                           source[:, k * P:(k + 1) * P], identf[:])
            last.then_inc(turned, 1)

        def multiply_item(item, j, weights):
            nc.tensor.wait_ge(lo_split, count(lo_split, item + 1))
            nc.tensor.wait_ge(z_lo, count(z_lo, slot_free(item, j)))
            n = 0
            for k in range(KC):
                for a, b in ((0, 0), (0, 1), (1, 0)):
                    last = nc.tensor.matmul(ps[:, ZB + j % 2, 0:D], outT[:, j % 2, a, k, :], weights[:, k, b, :],
                                            start=(n == 0), stop=(n == 3 * KC - 1))
                    n += 1
            last.then_inc(product, 1)

        def split_item_hi(item, j, tb=TB):
            nc.scalar.wait_ge(turned, count(turned, item + 1))
            nc.scalar.wait_ge(product, count(product, slot_free(item, j)))
            s = j % 2
            nc.scalar.activation(outT[:, s, 0].rearrange("p k c -> p (k c)"), ps[:, tb[s], 0:D],
                                 ACT.Copy).then_inc(hi_split, 1)

        def split_item_lo(item, j, tb=TB):
            s = j % 2
            nc.vector.wait_ge(hi_split, count(hi_split, item + 1))
            nc.vector.tensor_tensor(out=outT[:, s, 1].rearrange("p k c -> p (k c)"), in0=ps[:, tb[s], 0:D],
                                    in1=outT[:, s, 0].rearrange("p k c -> p (k c)"),
                                    op=ALU.subtract).then_inc(lo_split, 1)

        def keep_item_hi(item, j, dest):
            nc.scalar.wait_ge(product, count(product, item + 1))
            nc.scalar.activation(dest[:, 0:D], ps[:, ZB + j % 2, 0:D], ACT.Copy).then_inc(z_hi, 1)

        def keep_item_lo(item, j, dest):
            nc.vector.wait_ge(z_hi, count(z_hi, item + 1))
            nc.vector.tensor_tensor(out=dest[:, D:2 * D], in0=ps[:, ZB + j % 2, 0:D], in1=dest[:, 0:D],
                                    op=ALU.subtract).then_inc(z_lo, 1)

        def z_of_last_block(parity, it):
            if parity:
                return G * it + NB - 1
            block_no = G * it - 1 + 2 * NB * ((G - 1 - it) >> 2)
            return block_no if isinstance(block_no, int) else block_no.with_bounds(min_val=0, max_val=2 * NB - 1)

        @block.scalar
        def _(act):
            start(act, hi_split, z_hi, cnt_copied, wgt_hi, wadjT_copied, relu_done, base_written)
            for s in range(3):
                start(act, *wh_made[s], *wl_made[s][WL_DVE:])
            act.wait_ge(w0_turned, 1)
            for k in range(KC):
                last = nc.scalar.activation(w0T[:, k, 0, :], ps[:, AGG + k, 0:D], ACT.Copy)
            last.then_inc(w0_copied, 1)
            for i in range(NB + 1):
                if i < NB:
                    split_item_hi(i, i % G)
                if i > 0:
                    keep_item_hi(i - 1, (i - 1) % G, y[:, y_at(i - 1):y_at(i - 1) + 2].rearrange("p c f -> p (c f)"))
            act.wait_ge(bounds_made, 1)
            regs = window_registers(act, "act_window")

            def weight_rows(pair, side, window):
                def one_step(s, before, this, step):
                    for q in range(Q):
                        rows = lo_rows[s]
                        act.wait_ge(lo_made[s][q], this)
                        nc.scalar.activation(rows[:, q, 1, :], rows[:, q, 0, :], ACT.Copy,
                                             scale=scal[:, s, q, 2:3]).then_inc(wh_made[s][q], 1)
                        if q >= WL_DVE:
                            nc.scalar.activation(rows[:, q, 2, :], rows[:, q, 0, :], ACT.Copy,
                                                 scale=scal[:, s, q, 3:4]).then_inc(wl_made[s][q], 1)

                all_steps(act, pair, side, window, one_step)

            def copy_window(d, slot, column, pair, side, end):
                act.wait_ge(rows_used[side][Q - 1], pair + 2)
                act.wait_ge(rows_used[FURTHER][Q - 1], end + 1)
                nc.scalar.activation(wadj[slot][:, 0, :, bass.ds(column, WIN)],
                                     ps[:, WGT + side, 0:NB * WIN].rearrange("p (b j) -> p b j", j=WIN),
                                     ACT.Copy).then_inc(wgt_hi, 1)
                nc.scalar.activation(adj[:, d, :, bass.ds(column, WIN)],
                                     ps[:, CNT + side, 0:NB * WIN].rearrange("p (b j) -> p b j", j=WIN),
                                     ACT.Copy).then_inc(cnt_copied, 1)

            def copy_pair(d, q):
                n = min(2, NB - 2 * q)
                act.wait_ge(wadj_turned, count(wadj_turned, d * NPAIR + q + 1))
                act.wait_ge(l0_done, count(l0_done, d * NPAIR + max(q - 1, 0)))
                nc.scalar.activation(wadjT[:, q % 2, 0:n], trh[q % 2][:, 0:n], ACT.Copy).then_inc(wadjT_copied, 1)

            def block_windows(d, slot, lagging):
                if lagging:
                    act.wait_ge(l0_done, count(l0_done, (d - 1) * NPAIR))
                for k in range(0, WPB, 2):
                    odd, even = load_windows(act, regs, d * WPB + k + 1)
                    for side, window in ((0, odd), (1, even)):
                        pair = d * (WPB // 2) + k // 2
                        if lagging:
                            copy_window(d, slot, (k + side) * WIN, pair, side, window[0])
                            weight_rows(pair + side, 1 - side, window)
                        else:
                            weight_rows(pair + side, 1 - side, window)
                            copy_window(d, slot, (k + side) * WIN, pair, side, window[0])
                        if lagging:
                            for q in PAIRS[k + side]:
                                copy_pair(d - 1, q)

            weight_rows(0, 0, load_windows(act, regs, 0, 1)[0])
            block_windows(0, 0, False)
            with act.Fori(0, LAG // 2) as two:
                for s in (1, 2):
                    block_windows(two * 2 + s, s % 2, True)
            for q in range(NPAIR):
                copy_pair(LAG, q)
            with act.Fori(LAG + 1, NB) as d:
                block_windows(d, 0, False)
                for q in range(NPAIR):
                    copy_pair(d, q)
            act.wait_ge(w1_in, 16)
            act.wait_ge(wgt_copied, count(wgt_copied, NW))
            act.wait_ge(rows_used[0][Q - 1], NWP // 2 + 1)
            nc.scalar.activation(w1s[:, :, 0, :], w1, ACT.Copy).then_inc(w1_copied, 1)

            def deviations(n):
                act.wait_ge(var_ready, n)
                nc.scalar.activation(ln[:, 1, :], ln[:, 0, :], ACT.Sqrt).then_inc(std_ready, 1)

            def keep_base(item, j, block_no, first):
                if not first:
                    act.wait_ge(base_stored[j], 16 * first_it[0])
                act.wait_ge(product, count(product, item + 1))
                nc.scalar.activation(base_ring[:, j, :], ps[:, ZB + j % 2, 0:D], ACT.Copy,
                                     scale=ALPHA).then_inc(base_written, 1)
                keep_item_hi(item, j, z[:, block_no, :])

            first_it = [0]
            deviations(1)
            for i in range(NB + 1):
                if i % G == 0 and i // G + 1 < NB // G:
                    deviations(i // G + 2)
                if i < NB:
                    split_item_hi(NB + i, i % G)
                if i > 0:
                    first_it[0] = (i - 1) // G
                    keep_base(NB + i - 1, (i - 1) % G, i - 1, i <= G)

            def item_before(layer, parity, it, j):
                item = (layer + 2) * NB + it * G + j
                split_item_hi(item, j, TB_LAYERS)
                dest = z[:, z_of_last_block(parity, it), :] if j == 0 else z[:, parity * NB + it * G + j - 1, :]
                keep_item_hi(item, j, dest)

            def layer_blocks(layer, parity, it):
                for j in range(G):
                    g = layer * NB + it * G + j
                    item_before(layer, parity, it, j)
                    act.wait_ge(agg_read, count(agg_read, g + 1))
                    nc.scalar.activation(outb[:], pre[:], ACT.Relu).then_inc(relu_done, 1)

            act.wait_ge(x1_ready, count(x1_ready, NB))
            nc.scalar.activation(outb[:], h[:, NB - 1, :], ACT.Copy).then_inc(relu_done, 1)
            act.wait_ge(x1_stored, 16 * (NB // G))
            with act.Fori(0, LAYERS // 2) as pair:
                for odd in range(2):
                    with act.Fori(0, NB // G) as it:
                        layer_blocks(pair * 2 + odd, 1 - odd, it)
            item_before(LAYERS - 1, 1, 0, 0)
            for g in range(NB // G):
                deviations(NB // G + g + 1)

        @block.vector
        def _(dve):
            start(dve, lo_split, z_lo, wgt_copied, l0_added, deg_read, scale_made, agg_read)
            for s in range(3):
                start(dve, *lo_made[s], *key_made[s], *wl_made[s][:WL_DVE])
            nc.vector.memset(tab[:, NCH:NCHP, :], -float(2 ** 20)).then_inc(dve_consts, 1)
            chain = [0]

            def link(ins):
                chain[0] += 1
                ins.then_inc(dve_chain, 1)
                dve.wait_ge(dve_chain, chain[0])

            nc.vector.memset(ones16[:], 1.0).then_inc(dve_consts, 1)
            nc.vector.memset(steps_row[:], 1.0).then_inc(dve_consts, 1)
            nc.vector.memset(bounds[:], NCH).then_inc(dve_consts, 1)
            dve.wait_ge(edges_in, 6 * 16)
            dve.wait_ge(dve_consts, 4)
            nc.vector.tensor_scalar(src_lo[0:NR], src_raw[0:NR], P - 1, None, ALU.bitwise_and)
            nc.vector.tensor_scalar(dst_win[0:NR], dst_raw[0:NR], 4, None, ALU.logical_shift_right)
            link(nc.vector.tensor_scalar(src_hi[0:NR], src_raw[0:NR], 7, None, ALU.logical_shift_right))
            nc.vector.tensor_copy(src_lo_f[0:NR], src_lo[0:NR])
            nc.vector.tensor_reduce(chunk_rng[0:NR, 0], dst_win[0:NR].rearrange("p (t e) -> p t e", t=4), axis=AX.X, op=ALU.min)
            nc.vector.tensor_reduce(chunk_rng[0:NR, 1], dst_win[0:NR].rearrange("p (t e) -> p t e", t=4), axis=AX.X, op=ALU.max)
            link(nc.vector.scalar_tensor_tensor(out=key_f[0:NR], in0=dst_raw[0:NR], scalar=float(KM), in1=src_hi[0:NR],
                                                op0=ALU.mult, op1=ALU.add))
            nc.vector.nop().then_inc(edges_split, 1)
            for m in range(2):
                for t in range(4):
                    last = nc.vector.tensor_scalar(rng_rows[0:NR, m, t, :], ones16[0:NR], chunk_rng[0:NR, m, t:t + 1],
                                                   None, ALU.mult)
            last.then_inc(rows_made, 1)
            dve.wait_ge(edges_turned, 1)

            def turned_edges(n):
                return ps[:, n, 0:NCH].rearrange("p (t r) -> p r t", t=4)

            tables = tab[:, 0:NCH, :].rearrange("p (r t) k -> p r t k", t=4)
            link(nc.vector.tensor_copy(wh16[:], turned_edges(2)))
            nc.vector.tensor_copy(tables[:, :, :, 0], turned_edges(0))
            nc.vector.tensor_copy(tables[:, :, :, 1], turned_edges(1))
            nc.vector.tensor_copy(tables[:, :, :, 2], wh16[:])
            link(nc.vector.tensor_tensor(out=tables[:, :, :, 3], in0=turned_edges(2), in1=wh16[:], op=ALU.subtract))
            dve.wait_ge(rows_spread, 1)
            dve.wait_ge(consts_made, 8)
            for g in range(2):
                link(nc.vector.tensor_scalar(active[:, g, :], ps[:, 3, 0:NCH], win_no[:, g:g + 1], None, ALU.is_le))
                link(nc.vector.scalar_tensor_tensor(out=active[:, g, :], in0=ps[:, 4, 0:NCH], scalar=win_no[:, g:g + 1],
                                                    in1=active[:, g, :], op0=ALU.is_ge, op1=ALU.mult))
                for m, op in ((0, ALU.min), (1, ALU.max)):
                    link(nc.vector.tensor_tensor(out=cand[:, m, :], in0=active[:, g, :],
                                                 in1=chunk_no[:, m].rearrange("p t r -> p (t r)"), op=ALU.mult))
                    link(nc.vector.tensor_reduce(win_rng[:, g, m:m + 1], cand[:, m, :], axis=AX.X, op=op))
            link(nc.vector.tensor_scalar(win_rng[:, :, 0], win_rng[:, :, 0], float(NCH), float(NCH - 1), ALU.add, ALU.min))
            link(nc.vector.tensor_scalar(cand[:, 0, 0:2], win_rng[:, :, 0], 1.0, None, ALU.add))
            link(nc.vector.tensor_tensor(out=win_rng[:, :, 1], in0=win_rng[:, :, 1], in1=cand[:, 0, 0:2], op=ALU.max))
            link(nc.vector.tensor_copy(win_rng16[:], win_rng[:]))
            nc.vector.nop().then_inc(win_found, 1)
            dve.wait_ge(win_turned, 1)
            link(nc.vector.tensor_copy(win_row[:], ps[0:1, 5, 0:2 * NW].rearrange("p (m w) -> p m w", m=2)))
            n_steps, ends = steps_row[:, 0, 0:NW], steps_row[:, 1, :]
            link(nc.vector.tensor_tensor(out=n_steps, in0=win_row[:, 1, :], in1=win_row[:, 0, :], op=ALU.subtract))
            link(nc.vector.tensor_scalar(n_steps, n_steps, 1.0 / Q, (Q - 1) / 2 / Q, ALU.mult, ALU.add))
            link(nc.vector.tensor_scalar(n_steps, n_steps, ROUND, None, ALU.add))
            link(nc.vector.tensor_scalar(n_steps, n_steps, ROUND, None, ALU.subtract))
            further = steps_row[:, 0, :]
            link(nc.vector.tensor_scalar(further, further, 1.0, None, ALU.subtract))
            link(nc.vector.tensor_tensor_scan(out=ends, data0=steps_row[:, 2, :], data1=further, initial=0.0,
                                              op0=ALU.mult, op1=ALU.add))
            rows = bounds[:, 1:NWP + 1, :]
            nc.vector.tensor_tensor(out=rows[:, :, 0], in0=ends, in1=further, op=ALU.subtract)
            nc.vector.tensor_copy(rows[:, :, 1], ends)
            link(nc.vector.tensor_copy(rows[:, 0:NW, 2], win_row[:, 0, :]))
            nc.vector.nop().then_inc(bounds_made, 1)
            dve.wait_ge(w0_copied, 1)
            for k in range(KC):
                last = nc.vector.tensor_tensor(out=w0T[:, k, 1, :], in0=ps[:, AGG + k, 0:D], in1=w0T[:, k, 0, :], op=ALU.subtract)
            last.then_inc(w0_split, 1)
            for i in range(NB + 1):
                if i < NB:
                    split_item_lo(i, i % G)
                if i > 0:
                    keep_item_lo(i - 1, (i - 1) % G, y[:, y_at(i - 1):y_at(i - 1) + 2].rearrange("p c f -> p (c f)"))

            regs = window_registers(dve, "dve_window")

            def weights_lo(w, slot, column, side):
                dve.wait_ge(wgt_hi, count(wgt_hi, w + 1))
                nc.vector.tensor_tensor(out=wadj[slot][:, 1, :, bass.ds(column, WIN)],
                                        in0=ps[:, WGT + side, 0:NB * WIN].rearrange("p (b j) -> p b j", j=WIN),
                                        in1=wadj[slot][:, 0, :, bass.ds(column, WIN)],
                                        op=ALU.subtract).then_inc(wgt_copied, 1)

            def onehot_steps(pair, side, window):
                def one_step(s, before, this, step):
                    rows = lo_rows[s]
                    for q in range(Q):
                        dve.wait_ge(rows_used[s][q], before)
                        dve.wait_ge(scal_ready[s][q], this)
                        nc.vector.tensor_scalar(rows[:, q, 0, :], iota_lo[:], scal[:, s, q, 1:2], None,
                                                ALU.is_equal).then_inc(lo_made[s][q], 1)
                        nc.vector.tensor_scalar(key_rows[s][:, q], iota_key[:], scal[:, s, q, 0:1], None,
                                                ALU.is_equal).then_inc(key_made[s][q], 1)
                    for q in range(WL_DVE):
                        dve.wait_ge(lo_made[s][q], this)
                        nc.vector.tensor_scalar(rows[:, q, 2, :], rows[:, q, 0, :], scal[:, s, q, 3:4], None,
                                                ALU.mult).then_inc(wl_made[s][q], 1)

                all_steps(dve, pair, side, window, one_step)

            def add_pair(d, q):
                n = min(2, NB - 2 * q)
                dve.wait_ge(l0_done, count(l0_done, d * NPAIR + q + 1))
                nc.vector.tensor_tensor(out=h[:, 2 * q:2 * q + n, :],
                                        in0=ps[:, L0B + q % 2, 0:n * D].rearrange("p (b c) -> p b c", c=D),
                                        in1=h[:, 2 * q:2 * q + n, :], op=ALU.add).then_inc(l0_added, 1)

            def block_windows(d, slot, lagging):
                for k in range(0, WPB, 2):
                    w = d * WPB + k
                    odd, even = load_windows(dve, regs, w + 1)
                    for side, window in ((0, odd), (1, even)):
                        onehot_steps(d * (WPB // 2) + k // 2 + side, 1 - side, window)
                        weights_lo(w + side, slot, (k + side) * WIN, side)
                        if lagging and k + side > 0:
                            for q in PAIRS[k + side - 1]:
                                add_pair(d - 1, q)
                if lagging:
                    for q in PAIRS[WPB - 1]:
                        add_pair(d - 1, q)

            onehot_steps(0, 0, load_windows(dve, regs, 0, 1)[0])
            block_windows(0, 0, False)
            with dve.Fori(0, LAG // 2) as two:
                for s in (1, 2):
                    block_windows(two * 2 + s, s % 2, True)
            for q in range(NPAIR):
                add_pair(LAG, q)
            with dve.Fori(LAG + 1, NB) as d:
                block_windows(d, 0, False)
                for q in range(NPAIR):
                    add_pair(d, q)
            nc.vector.memset(z[:, 0:NB, 2 * D:ZW], 1.0)

            def layernorm_group(g, n):
                for j in range(G):
                    last = nc.vector.bn_stats(stat[:, j, :], h[:, g * G + j, :])
                link(last)
                for j in range(G):
                    last = nc.vector.bn_aggr(mean_var[:, g * G + j, :], stat[:, j, :])
                link(last)
                nc.vector.tensor_scalar(ln[:, 0, :], mean_var[:, g * G:(g + 1) * G, 1], EPS, None, ALU.add).then_inc(var_ready, 1)
                dve.wait_ge(std_ready, n)
                r = rstd[:, g * G:(g + 1) * G]
                link(nc.vector.reciprocal(ln[:, 2, :], ln[:, 1, :]))
                link(nc.vector.tensor_tensor(out=ln[:, 3, :], in0=ln[:, 2, :], in1=ln[:, 2, :], op=ALU.mult))
                link(nc.vector.tensor_tensor(out=ln[:, 3, :], in0=ln[:, 3, :], in1=ln[:, 0, :], op=ALU.mult))
                link(nc.vector.tensor_scalar(ln[:, 3, :], ln[:, 3, :], -0.5, 1.5, ALU.mult, ALU.add))
                return nc.vector.tensor_tensor(out=r, in0=ln[:, 3, :], in1=ln[:, 2, :], op=ALU.mult)

            dve.wait_ge(l0_added, count(l0_added, NB * NPAIR))
            layernorm_group(0, 1).then_inc(rstd_made, 1)
            dve.wait_ge(w1_copied, 1)
            nc.vector.tensor_tensor(out=w1s[:, :, 1, :], in0=w1, in1=w1s[:, :, 0, :], op=ALU.subtract).then_inc(w1_split, 1)
            for i in range(NB + 1):
                if i % G == 0 and i // G + 1 < NB // G:
                    layernorm_group(i // G + 1, i // G + 2).then_inc(rstd_made, 1)
                if i < NB:
                    split_item_lo(NB + i, i % G)
                if i > 0:
                    keep_item_lo(NB + i - 1, (i - 1) % G, z[:, i - 1, :])

            def item_before(layer, parity, it, j):
                item = (layer + 2) * NB + it * G + j
                split_item_lo(item, j, TB_LAYERS)
                dest = z[:, z_of_last_block(parity, it), :] if j == 0 else z[:, parity * NB + it * G + j - 1, :]
                keep_item_lo(item, j, dest)

            def scaled(layer, it, j):
                g = layer * NB + it * G + j
                dve.wait_ge(agg_done, count(agg_done, g + 1))
                nc.vector.tensor_scalar(scale[:, 0:1], ps[:, AGG + j, D:D + 1], 1.0, 1 / (1 - ALPHA), ALU.max,
                                        ALU.mult).then_inc(deg_read, 1)
                dve.wait_ge(deg_read, count(deg_read, g + 1))
                nc.vector.reciprocal(scale[:, 1:2], scale[:, 0:1]).then_inc(scale_made, 1)
                dve.wait_ge(scale_made, count(scale_made, g + 1))
                dve.wait_ge(base_loaded[j], 16 * (layer * (NB // G) + it + 1))
                return nc.vector.scalar_tensor_tensor(out=pre[:], in0=ps[:, AGG + j, 0:D], scalar=scale[:, 1:2],
                                                      in1=base_ring[:, j, :], op0=ALU.mult, op1=ALU.add)

            dve.wait_ge(x1_stored, 16 * (NB // G))
            dve.wait_ge(relu_done, count(relu_done, 1))
            nc.vector.memset(z[:, NB:2 * NB, 2 * D:ZW], 1.0).then_inc(ones_made, 1)
            with dve.Fori(0, LAYERS // 2) as pair:
                for odd in range(2):
                    layer = pair * 2 + odd
                    with dve.Fori(0, NB // G) as it:
                        for j in range(G):
                            item_before(layer, 1 - odd, it, j)
                            dve.wait_ge(relu_done, count(relu_done, layer * NB + it * G + j + 1))
                            scaled(layer, it, j).then_inc(agg_read, 1)
            item_before(LAYERS - 1, 1, 0, 0)
            dve.wait_ge(relu_done, count(relu_done, (LAYERS - 1) * NB + 1))
            dve.wait_ge(x1_loaded, 16)
            for it in range(NB // G):
                for j in range(G):
                    ins = scaled(LAYERS - 1, it, j)
                    ins.then_inc(agg_read, 1)
                    dve.wait_ge(agg_read, count(agg_read, (LAYERS - 1) * NB + it * G + j + 1))
                    link(nc.vector.scalar_tensor_tensor(out=h[:, it * G + j, :], in0=pre[:], scalar=0.0,
                                                        in1=h[:, it * G + j, :], op0=ALU.max, op1=ALU.add))
                link(layernorm_group(it, NB // G + it + 1))
                for i in range(it * G, (it + 1) * G):
                    last = nc.vector.tensor_scalar(h[:, i, :], h[:, i, :], mean_var[:, i, 0:1], rstd[:, i:i + 1],
                                                   ALU.subtract, ALU.mult)
                last.then_inc(normed, 1)

        @block.tensor
        def _(pe):
            start(pe, turned, product, wadj_turned, l0_done, agg_done, *rows_used[0], *rows_used[1], *rows_used[2])
            pe.wait_ge(consts_made, 8)
            pe.wait_ge(edges_split, 1)
            for n, table in enumerate((key_f, src_lo_f, wgt_raw)):
                for t in range(4):
                    last = nc.tensor.transpose(ps[:, n, t * NR:(t + 1) * NR], table[0:NR, t * P:(t + 1) * P], identf[0:NR, 0:NR])
            last.then_inc(edges_turned, 1)
            pe.wait_ge(rows_made, 1)
            for m in range(2):
                for t in range(4):
                    last = nc.tensor.matmul(ps[:, 3 + m, t * NR:(t + 1) * NR], rng_rows[0:NR, m, t, :], identh[0:NR, 0:NR],
                                            start=True, stop=True)
            last.then_inc(rows_spread, 1)
            pe.wait_ge(win_found, 1)
            for m in range(2):
                for g in range(2):
                    last = nc.tensor.matmul(ps[0:1, 5, m * NW + g * HW:m * NW + (g + 1) * HW], win_rng16[0:HW, g, m:m + 1],
                                            identh[0:HW, 0:HW], start=True, stop=True)
            last.then_inc(win_turned, 1)
            pe.wait_ge(w0_in, 16)
            for k in range(KC):
                for c in range(KC):
                    last = nc.tensor.transpose(ps[:, AGG + k, c * P:(c + 1) * P], w0[:, c, k * P:(k + 1) * P], identf[:])
            last.then_inc(w0_turned, 1)
            pe.wait_ge(bounds_made, 1)
            pe.wait_ge(w0_split, 1)
            pe.wait_ge(x_in, 32)
            for i in range(NB + 1):
                if i < NB:
                    turn_item(i, i % G, h[:, i, :])
                if i > 0:
                    multiply_item(i - 1, (i - 1) % G, w0T)
            pe.wait_ge(z_lo, count(z_lo, NB))
            pe.wait_ge(bias_added, NB)

            regs = window_registers(pe, "pe_window")

            def window_products(w, pair, side, window):
                pe.wait_ge(cnt_copied, w + 1)
                pe.wait_ge(wgt_copied, w + 1)
                for bank in (CNT + side, WGT + side):
                    nc.tensor.matmul(ps[:, bank, NB * WIN:NB * WIN + 1], identh[:], identh[:, 0:1],
                                     start=True, stop=True, skip_group_check=True)

                def one_step(s, before, this, step):
                    for q in range(Q):
                        keys = key_rows[s][:, q].rearrange("p b j -> p (b j)")
                        pe.wait_ge(key_made[s][q], this)
                        nc.tensor.matmul(ps[:, CNT + side, 0:NB * WIN], lo_rows[s][:, q, 0, :], keys,
                                         start=False, stop=True, skip_group_check=True)
                        pe.wait_ge(wh_made[s][q], this)
                        nc.tensor.matmul(ps[:, WGT + side, 0:NB * WIN], lo_rows[s][:, q, 1, :], keys,
                                         start=False, stop=True, skip_group_check=True)
                        pe.wait_ge(wl_made[s][q], this)
                        nc.tensor.matmul(ps[:, WGT + side, 0:NB * WIN], lo_rows[s][:, q, 2, :], keys,
                                         start=False, stop=True, skip_group_check=True).then_inc(rows_used[s][q], 1)

                all_steps(pe, pair, side, window, one_step)

            def turn_weights(d, slot, q):
                pe.wait_ge(wadjT_copied, count(wadjT_copied, d * NPAIR + max(q - 1, 0)))
                for b in range(2 * q, min(2 * q + 2, NB)):
                    for half in range(2):
                        last = nc.tensor.transpose(trh[q % 2][:, b % 2, half, :], wadj[slot][:, half, b, :], identh[:])
                last.then_inc(wadj_turned, 1)

            def multiply_weights(d, q):
                pe.wait_ge(wadjT_copied, count(wadjT_copied, d * NPAIR + q + 1))
                pe.wait_ge(l0_added, count(l0_added, d * NPAIR + max(q - 1, 0)))
                for b in range(2 * q, min(2 * q + 2, NB)):
                    to = ps[:, L0B + q % 2, (b % 2) * D:(b % 2 + 1) * D]
                    for n, (a, c) in enumerate(((0, 0), (0, 1), (1, 0))):
                        last = nc.tensor.matmul(to, wadjT[:, q % 2, b % 2, a, :], y[:, y_at(d) + c, :],
                                                start=(n == 0), stop=(n == 2))
                last.then_inc(l0_done, 1)

            def block_windows(d, slot, lagging):
                for k in range(0, WPB, 2):
                    w = d * WPB + k
                    odd, even = load_windows(pe, regs, w + 1)
                    for side, window in ((0, odd), (1, even)):
                        if lagging:
                            if k + side == 0:
                                pe.wait_ge(wgt_copied, count(wgt_copied, d * WPB))
                            for q in PAIRS[k + side]:
                                turn_weights(d - 1, 1 - slot, q)
                        window_products(w + side + 1, d * (WPB // 2) + k // 2 + side, 1 - side, window)
                        if lagging:
                            for q in PAIRS[k + side]:
                                multiply_weights(d - 1, q)

            def block_pairs(d):
                pe.wait_ge(wgt_copied, count(wgt_copied, (d + 1) * WPB))
                for q in range(NPAIR + 1):
                    if q < NPAIR:
                        turn_weights(d, 0, q)
                    if q > 0:
                        multiply_weights(d, q - 1)

            window_products(0, 0, 0, load_windows(pe, regs, 0, 1)[0])
            block_windows(0, 0, False)
            with pe.Fori(0, LAG // 2) as two:
                for s in (1, 2):
                    block_windows(two * 2 + s, s % 2, True)
            block_pairs(LAG)
            with pe.Fori(LAG + 1, NB) as d:
                block_windows(d, 0, False)
                block_pairs(d)
            pe.wait_ge(l0_added, count(l0_added, NB * NPAIR))
            pe.wait_ge(w1_split, 1)
            for i in range(NB + 1):
                if i < NB:
                    pe.wait_ge(x1_ready, count(x1_ready, i + 1))
                    turn_item(NB + i, i % G, h[:, i, :])
                if i > 0:
                    multiply_item(NB + i - 1, (i - 1) % G, w1s)

            def layer_block(layer, parity, it, j, item_too):
                g = layer * NB + it * G + j
                item = (layer + 2) * NB + it * G + j
                pe.wait_ge(agg_read, g + 1)
                pe.wait_ge(z_lo, count(z_lo, (layer + 2) * NB))
                for b in range(NB):
                    if b == 10 and item_too:
                        pe.wait_ge(relu_done, count(relu_done, g + 1))
                        turn_item(item, j, outb, TB_LAYERS)
                    if b == 18 and item_too:
                        multiply_item(item, j, w1s)
                    if b == NB - 1:
                        pe.wait_ge(z_lo, count(z_lo, (layer + 2) * NB + 1))
                    for half in range(2):
                        width = D + half
                        last = nc.tensor.matmul(ps[:, AGG + j, 0:width], adj[:, it * G + j, b, :],
                                                z[:, (1 - parity) * NB + b, half * D:half * D + width],
                                                start=(b == 0 and half == 0), stop=(b == NB - 1 and half == 1),
                                                skip_group_check=True)
                last.then_inc(agg_done, 1)

            pe.wait_ge(ones_made, 1)
            with pe.Fori(0, LAYERS // 2) as pair:
                for odd in range(2):
                    with pe.Fori(0, NB // G) as it:
                        for j in range(G):
                            layer_block(pair * 2 + odd, 1 - odd, it, j, True)
            for j in range(G):
                layer_block(LAYERS - 1, 1, 0, j, j == 0)
            with pe.Fori(1, NB // G) as it:
                for j in range(G):
                    layer_block(LAYERS - 1, 1, it, j, False)


_INS = ["x", "src", "dst", "edge_weight", "L0_gnn_W", "L0_gnn_b", "L1_gnn_W"]


def kernel(**inputs):
    import numpy as _np
    import concourse.bacc as _bacc
    from concourse import mybir as _mybir
    from concourse.bass_utils import run_bass_kernel_spmd as _run

    nc = _bacc.Bacc("TRN2", target_bir_lowering=False, num_devices=1, dynamic_dma_scratch_size=1024)
    arrays, args = {}, []
    for name in _INS:
        a = _np.ascontiguousarray(inputs[name])
        arrays[f"in_{name}"] = a
        args.append(nc.dram_tensor(f"in_{name}", a.shape, _mybir.dt.from_np(a.dtype), kind="ExternalInput").ap())
    out = nc.dram_tensor("result", inputs["x"].shape, _mybir.dt.float32, kind="ExternalOutput").ap()
    gnn_resnorm_kernel(nc, *args, out)
    r = _run(nc, [arrays], core_ids=[0])
    return r.results[0]["result"]
```
